# Optimizing a Trainium2 kernel written in Bass

```python
import numpy as np
import jax
import jax.numpy as jnp

def _softmax(x, axis=-1):
    return jax.nn.softmax(x, axis=axis)

def _gelu(x):
    return jax.nn.gelu(x, approximate=True)

def _silu(x):
    return jax.nn.silu(x)

def _sigmoid(x):
    return jax.nn.sigmoid(x)

def _layernorm(x, axis=-1, eps=1e-05):
    m = jnp.mean(x, axis=axis, keepdims=True)
    v = jnp.var(x, axis=axis, keepdims=True)
    return (x - m) / jnp.sqrt(v + eps)

def _scatter_add(tgt, idx, src, axis=0):
    return tgt.at[idx].add(src)

def _segment_sum(src, seg, n):
    return jax.ops.segment_sum(src, seg, n)
kernel_name = 'mk_adj_preln_d2_adj_r2_33d497'

def setup_inputs(seed: int=0):
    np.random.seed(seed)
    _w = jnp.asarray

    def _rec_inputs():
        import jax
        import jax.numpy as jnp
        _gk = jax.random.key(seed)
        x = -0.0005207 + 1.001 * jax.random.normal(jax.random.fold_in(_gk, 1), (8192, 128), jnp.float32)
        _a = jax.random.bernoulli(jax.random.fold_in(_gk, 2), 0.000244141, (8192, 8192))
        _a = jnp.logical_or(_a, jnp.swapaxes(_a, -1, -2))
        _a = jnp.logical_or(_a, jnp.eye(8192, dtype=bool))
        _af = _a.astype(jnp.float32)
        _af = _af * jax.random.uniform(jax.random.fold_in(_gk, 3), (8192, 8192), jnp.float32, 0.05, 1)
        adj = _af
        return (x, adj)
    x, adj = _rec_inputs()

    def _L0_gnn_setup():
        import jax, jax.numpy as jnp
        import numpy as np
        N = 8192
        F_IN = 128
        F_OUT = 128
        key = jax.random.key(seed)
        k1, k2, k3, k4 = jax.random.split(key, 4)
        x = jax.random.normal(k1, (N, F_IN), dtype=jnp.float32)
        adj = jax.random.uniform(k2, (N, N), dtype=jnp.float32)
        bound = 1.0 / np.sqrt(2 * F_IN)
        W = jax.random.uniform(k3, (F_OUT, 2 * F_IN), minval=-bound, maxval=bound, dtype=jnp.float32)
        b = jax.random.uniform(k4, (F_OUT,), minval=-bound, maxval=bound, dtype=jnp.float32)
        return {'x': x, 'adj': adj, 'W': W, 'b': b}
    _L0_gnn_all = _L0_gnn_setup()
    _L0_gnn_in = {k: v for k, v in _L0_gnn_all.items() if k in ('W', 'b')}
    del _L0_gnn_all

    def _L1_gnn_setup():
        import jax, jax.numpy as jnp
        import numpy as np
        N = 4096
        D = 128
        key = jax.random.key(seed)
        kx, ka, kw1, kw2 = jax.random.split(key, 4)
        x = jax.random.normal(kx, (N, D), dtype=jnp.float32)
        A = jax.random.uniform(ka, (N, N), dtype=jnp.float32)
        s = 0.05
        W1 = jax.random.normal(kw1, (D, D), dtype=jnp.float32) * s
        b1 = jnp.zeros((D,), dtype=jnp.float32)
        W2 = jax.random.normal(kw2, (D, D), dtype=jnp.float32) * s
        b2 = jnp.zeros((D,), dtype=jnp.float32)
        return {'x': x, 'A': A, 'W1': W1, 'b1': b1, 'W2': W2, 'b2': b2}
    _L1_gnn_all = _L1_gnn_setup()
    _L1_gnn_in = {k: v for k, v in _L1_gnn_all.items() if k in ('W1', 'b1', 'W2', 'b2')}
    del _L1_gnn_all
    return {'x': x, 'adj': adj, 'L0_gnn_W': _L0_gnn_in['W'], 'L0_gnn_b': _L0_gnn_in['b'], 'L1_gnn_W1': _L1_gnn_in['W1'], 'L1_gnn_b1': _L1_gnn_in['b1'], 'L1_gnn_W2': _L1_gnn_in['W2'], 'L1_gnn_b2': _L1_gnn_in['b2']}

def reference(x, adj, L0_gnn_W, L0_gnn_b, L1_gnn_W1, L1_gnn_b1, L1_gnn_W2, L1_gnn_b2):
    import jax
    import jax.numpy as jnp

    def _L0_gnn_ref(x, adj, W, b):
        import jax, jax.numpy as jnp
        import numpy as np
        N = 8192
        F_IN = 128
        F_OUT = 128
        neigh = adj @ x
        W_self = W[:, :F_IN]
        W_neigh = W[:, F_IN:]
        return x @ W_self.T + neigh @ W_neigh.T + b

    def _L1_gnn_ref(x, A, W1, b1, W2, b2):
        import jax, jax.numpy as jnp
        import numpy as np
        N = 4096
        D = 128
        h = jax.nn.relu(jnp.matmul(A, jnp.matmul(x, W1)) + b1)
        h = jax.nn.relu(jnp.matmul(A, jnp.matmul(h, W2)) + b2)
        return h
    h = jnp.maximum(_layernorm(x, axis=-1), 0.0)
    x = x + _L0_gnn_ref(h, adj, L0_gnn_W, L0_gnn_b)
    h = jnp.maximum(_layernorm(x, axis=-1), 0.0)
    x = x + _L1_gnn_ref(h, adj, L1_gnn_W1, L1_gnn_b1, L1_gnn_W2, L1_gnn_b2)
    return x

_drawn_inputs = setup_inputs


def setup_inputs(seed=0):
    import zlib

    import numpy as np

    out = dict(_drawn_inputs(seed))
    spreads = {'L1_gnn_b1': (0.0, 0.1), 'L1_gnn_b2': (0.0, 0.1)}
    factors = {}
    for name, (base, spread) in spreads.items():
        noise = np.random.default_rng([zlib.crc32(name.encode()), seed]).standard_normal(out[name].shape)
        drawn = base * np.exp(spread * noise) if base else spread * noise
        out[name] = jnp.asarray(drawn.astype(out[name].dtype))
    for name, factor in factors.items():
        out[name] = (out[name] * factor).astype(out[name].dtype)
    return out
```

```python
from contextlib import ExitStack

import concourse.bass as bass
from concourse import mybir

F32 = mybir.dt.float32
F32R = mybir.dt.float32r
BF16 = mybir.dt.bfloat16
ALU = mybir.AluOpType
ACT = mybir.ActivationFunctionType

P = 128
N = 8192
F = 128
R = 1024
CHUNKS = N // R
BANK = 512
HALVES = R // BANK
SLABS = R // P
PER_TILE = 2
TILES = SLABS // PER_TILE
DEPTH = 4
HALF = SLABS // 2
EPS = 1e-5


def plan():
    chunks = []
    for i in range(CHUNKS):
        chunks.append((0, i, (i, 1, CHUNKS - i), (0, 1, i)))
    for i in reversed(range(CHUNKS)):
        chunks.append((1, i, (i, 1, 1), (CHUNKS - 1, -1, CHUNKS - 1 - i)))
    for i in reversed(range(CHUNKS)):
        chunks.append((2, i, (i, -1, i + 1), (0, 1, 0)))
    return chunks


LEAD = (0, 1, 0)
SIDE = (1, 0, None)


def g_count(sweep, j, of_side):
    which = sweep + (1 if of_side else 0)
    if which == 0:
        return 1 + j
    if which == 1:
        return CHUNKS + 1 + j
    return 3 * CHUNKS - j


def build(nc, adj_t, x_t, w0_t, b0, w1, b1, w2, b2, out_t):
    chunks = plan()
    starts = [0]
    for _, _, a, s in chunks:
        starts.append(starts[-1] + a[2] + s[2])
    sweep0_end = starts[CHUNKS]

    with ExitStack() as ctx:
        def sb(name, shape, dt=F32):
            return ctx.enter_context(nc.sbuf_tensor(name, shape, dt))

        def psum(name, shape):
            return ctx.enter_context(nc.psum_tensor(name, shape, F32))

        def sem(name):
            return ctx.enter_context(nc.semaphore(name))

        x1_dram = nc.dram_tensor("x1_t", [CHUNKS, F, R], F32, kind="Internal").ap()

        lead_acc = psum("lead_acc", [P, 2, R])
        side_acc = psum("side_acc", [P, R])
        work_ps = psum("work_ps", [P, R])

        g_all = sb("g_all", [P, 2, N])
        part = sb("part", [P, N])
        a_ring = sb("a_ring", [P, TILES, PER_TILE, R])
        a_high = sb("a_high", [P, DEPTH, R], F32R)
        a_rest = sb("a_rest", [P, DEPTH, R], F32R)
        g_high = sb("g_high", [P, 2, SLABS, F], F32R)
        g_rest = sb("g_rest", [P, 2, SLABS, F], F32R)
        x_buf = sb("x_buf", [P, 2, R])
        centred = sb("centred", [P, R])
        spread = sb("spread", [P, R])
        h_buf = sb("h_buf", [P, R])
        w0_sb = sb("w0_sb", [P, 2, F])
        w1_sb = sb("w1_sb", [P, F])
        w2_sb = sb("w2_sb", [P, F])
        biases = sb("biases", [P, 3])
        eps_col = sb("eps_col", [P, 1])
        mean_w = sb("mean_w", [P, F])
        zeros = sb("zeros", [P, P], BF16)

        consts_loaded = sem("consts_loaded")
        consts_set = sem("consts_set")
        tile_loaded = [sem(f"tile_loaded{v}") for v in range(TILES)]
        high_ready = sem("high_ready")
        rest_ready = sem("rest_ready")
        slab_used = sem("slab_used")
        x_loaded = [sem(f"x_loaded{p}") for p in range(2)]
        x1_ready = sem("x1_ready")
        x1_stored = [sem(f"x1_stored{p}") for p in range(2)]
        x1_back = [sem(f"x1_back{p}") for p in range(2)]
        mean_ready = sem("mean_ready")
        centred_ready = sem("centred_ready")
        squares_ready = sem("squares_ready")
        var_ready = sem("var_ready")
        dev_ready = sem("dev_ready")
        inv_ready = sem("inv_ready")
        normed = sem("normed")
        g_product = sem("g_product")
        g_saved = sem("g_saved")
        self_product = sem("self_product")
        base_saved = sem("base_saved")
        sum_ready = sem("sum_ready")
        side_saved = sem("side_saved")
        h_ready = sem("h_ready")
        out_ready = sem("out_ready")
        out_stored = sem("out_stored")

        block = ctx.enter_context(nc.Block())

        def cols(half):
            return slice(half * BANK, (half + 1) * BANK)

        def chunk_cols(i):
            return slice(i * R, (i + 1) * R)

        def side_chunks(c):
            return sum(1 for _, _, _, s in chunks[:c] if s[2])

        def run_chunk(eng, c, one_block, hooks=None, at_side=None):
            sweep, i, lead_part, side_part = chunks[c]
            hooks = hooks or {}
            n_peeled = 1 + max(hooks, default=-1) // SLABS if hooks else 0
            n = starts[c]
            done = 0
            for (j0, dj, count), shared in ((lead_part, False), (side_part, True)):
                if not count:
                    continue
                if shared and at_side:
                    at_side()
                t = 0
                g_first = g_count(sweep, j0, shared)
                while t < count and done < n_peeled:
                    one_block(j0 + dj * t, n, shared, g_first + t, {k - done * SLABS: f for k, f in hooks.items()
                                                       if done * SLABS <= k < (done + 1) * SLABS})
                    t, n, done = t + 1, n + 1, done + 1
                if count - t == 1:
                    one_block(j0 + dj * t, n, shared, g_first + t, {})
                elif count - t > 1:
                    with eng.Fori(0, count - t) as k:
                        j = (j0 + t) + k if dj > 0 else k * -1 + (j0 - t)
                        one_block(j, n + k, shared,
                                  g_first + t + k, {})
                n += count - t

        @block.sync
        def _(sp):
            def load_block(i, j, n, first=False):
                for v in range(TILES):
                    if not first:
                        sp.wait_ge(rest_ready, n * SLABS + (PER_TILE * (v + 1) - SLABS))
                    sp.dma_start(a_ring[:, v], adj_t[i, bass.ds(j * TILES + v, 1)].rearrange(
                        "o p s r -> p (o s) r")).then_inc(tile_loaded[v], 16)

            sp.dma_start(w0_sb[:], w0_t.rearrange("(s p) f -> p s f", p=P)).then_inc(consts_loaded, 16)
            sp.dma_start(w1_sb[:], w1).then_inc(consts_loaded, 16)
            sp.dma_start(w2_sb[:], w2).then_inc(consts_loaded, 16)
            for q, b in enumerate((b0, b1, b2)):
                sp.dma_start(biases[:, q:q + 1], b).then_inc(consts_loaded, 16)
            load_block(0, 0, 0, first=True)
            with sp.Fori(1, CHUNKS) as j:
                load_block(0, j, j)
            for c in range(1, len(chunks)):
                i = chunks[c][1]
                run_chunk(sp, c, lambda j, n, shared, g_needed, hook: load_block(i, j, n))

        @block.gpsimd
        def _(pool):
            nc.gpsimd.memset(mean_w[:], 1.0 / F)
            nc.gpsimd.memset(eps_col[:], EPS)
            nc.gpsimd.memset(zeros[:], 0.0).then_inc(consts_set, 1)
            for i in range(CHUNKS):
                if i >= 2:
                    pool.wait_ge(base_saved, i - 1)
                pool.dma_start(x_buf[:, i % 2], x_t[i]).then_inc(x_loaded[i % 2], 16)
            for i in range(CHUNKS):
                pool.wait_ge(x1_ready, i + 1)
                pool.dma_start(x1_dram[i], x_buf[:, i % 2]).then_inc(x1_stored[i % 2], 16)
            for p in range(2):
                pool.wait_ge(x1_stored[p], 16 * (CHUNKS // 2))
            for e, i in enumerate(reversed(range(CHUNKS))):
                if e < 2:
                    pool.wait_ge(centred_ready, 2 * CHUNKS)
                else:
                    pool.wait_ge(out_ready, e - 1)
                pool.dma_start(x_buf[:, i % 2], x1_dram[i]).then_inc(x1_back[i % 2], 16)
                if e >= 1:
                    pool.wait_ge(out_ready, e)
                    pool.dma_start(out_t[i + 1], h_buf[:]).then_inc(out_stored, 16)
            pool.wait_ge(out_ready, CHUNKS)
            pool.dma_start(out_t[0], h_buf[:]).then_inc(out_stored, 16)
            pool.wait_ge(out_stored, 16 * CHUNKS)

        @block.scalar
        def _(act):
            def squares(l):
                act.wait_ge(centred_ready, l + 1)
                nc.scalar.activation(spread[:], centred[:], ACT.Square).then_inc(squares_ready, 1)

            def deviation(l):
                act.wait_ge(var_ready, l + 1)
                nc.scalar.activation(spread[:], work_ps[:], ACT.Sqrt, bias=eps_col[:, 0:1]).then_inc(dev_ready, 1)

            def split_block(sweep, j, n, shared, g_needed, hook, first=False):
                for u in range(SLABS):
                    if u % PER_TILE == 0:
                        act.wait_ge(tile_loaded[u // PER_TILE], n * 16 + 16)
                    if not first or u >= DEPTH:
                        act.wait_ge(slab_used, n * SLABS + (u + 1 - DEPTH))
                    if u % HALF == 0:
                        a, b = (0, 2) if shared else (LEAD[sweep], LEAD[sweep] + 1)
                        if u == 0:
                            act.wait_ge(g_saved, g_needed)
                        nc.scalar.activation(
                            g_high[:, a:b, u:u + HALF].rearrange("p g s f -> p g (s f)"),
                            g_all[:, a:b, bass.ds(j * R + u * F, HALF * F)], ACT.Copy)
                    nc.scalar.activation(a_high[:, u % DEPTH], a_ring[:, u // PER_TILE, u % PER_TILE],
                                         ACT.Copy).then_inc(high_ready, 1)
                    if u in hook:
                        hook[u]()

            def save_side(c):
                sweep, i, _, side_part = chunks[c]
                if side_part[2]:
                    act.wait_ge(slab_used, SLABS * starts[c + 1])
                    if sweep == 1:
                        act.wait_ge(sum_ready, c + 1)
                    nc.scalar.activation(part[:, chunk_cols(i)], side_acc[:], ACT.Copy).then_inc(side_saved, 1)

            def relu(c):
                act.wait_ge(sum_ready, c + 1)
                e = c - 2 * CHUNKS
                if e >= 1:
                    act.wait_ge(out_stored, 16 * e)
                q = chunks[c][0]
                nc.scalar.activation(h_buf[:], centred[:], ACT.Relu, bias=biases[:, q:q + 1]).then_inc(h_ready, 1)

            act.wait_ge(consts_set, 1)
            for i in range(CHUNKS):
                squares(i)
                deviation(i)
            act.wait_ge(consts_loaded, 16 * 6)
            for c in range(len(chunks)):
                sweep = chunks[c][0]
                hooks = {}
                if 1 <= c < CHUNKS:
                    l = CHUNKS + c - 1
                    hooks = {5: lambda: save_side(c - 1), 7: lambda: squares(l), 11: lambda: deviation(l)}
                elif c > CHUNKS:
                    hooks = {4: lambda: relu(c - 1), 5: lambda: save_side(c - 1)}
                if c == CHUNKS:
                    save_side(c - 1)
                    squares(2 * CHUNKS - 1)
                    deviation(2 * CHUNKS - 1)
                if c == 0:
                    split_block(0, 0, 0, False, 1, {}, first=True)
                    with act.Fori(1, CHUNKS) as j:
                        split_block(0, j, j, False, j + 1, {})
                else:
                    run_chunk(act, c, lambda j, n, shared, g_needed, hook: split_block(
                        sweep, j, n, shared, g_needed, hook), hooks)
            relu(len(chunks) - 1)

        @block.vector
        def _(dve):
            def centre(l, source):
                dve.wait_ge(mean_ready, l + 1)
                nc.vector.tensor_tensor(centred[:], source, work_ps[:], ALU.subtract).then_inc(centred_ready, 1)

            def invert(l):
                dve.wait_ge(dev_ready, l + 1)
                nc.vector.reciprocal(spread[:], spread[:]).then_inc(inv_ready, 1)

            def norm(l):
                dve.wait_ge(inv_ready, l + 1)
                nc.vector.scalar_tensor_tensor(out=h_buf[:], in0=centred[:], scalar=0.0, in1=spread[:],
                                               op0=ALU.max, op1=ALU.mult).then_inc(normed, 1)

            def save_g(e, which, i):
                dve.wait_ge(g_product, e + 1)
                nc.vector.tensor_copy(g_all[:, which, chunk_cols(i)], work_ps[:]).then_inc(g_saved, 1)

            def split_block(sweep, j, n, shared, hook):
                for u in range(SLABS):
                    dve.wait_ge(high_ready, n * SLABS + (u + 1))
                    if u % HALF == 0:
                        a, b = (0, 2) if shared else (LEAD[sweep], LEAD[sweep] + 1)
                        nc.vector.tensor_tensor(
                            g_rest[:, a:b, u:u + HALF].rearrange("p g s f -> p g (s f)"),
                            g_all[:, a:b, bass.ds(j * R + u * F, HALF * F)],
                            g_high[:, a:b, u:u + HALF].rearrange("p g s f -> p g (s f)").bitcast(F32),
                            ALU.subtract)
                    nc.vector.tensor_tensor(a_rest[:, u % DEPTH], a_ring[:, u // PER_TILE, u % PER_TILE],
                                            a_high[:, u % DEPTH].bitcast(F32), ALU.subtract).then_inc(rest_ready, 1)
                    if u in hook:
                        hook[u]()

            def finish_sum(c):
                sweep, i, _, _ = chunks[c]
                dve.wait_ge(slab_used, SLABS * starts[c + 1])
                acc = lead_acc[:, c % 2]
                if sweep == 0:
                    if i < 2:
                        dve.wait_ge(base_saved, CHUNKS)
                    else:
                        dve.wait_ge(x1_stored[i % 2], 16 * (i // 2))
                    nc.vector.tensor_tensor(x_buf[:, i % 2], acc, g_all[:, 1, chunk_cols(i)], ALU.add
                                            ).then_inc(sum_ready, 1)
                    dve.wait_ge(sum_ready, c + 1)
                    nc.vector.engine_nop().then_inc(x1_ready, 1)
                elif (sweep == 1 and i == 0) or (sweep == 2 and i == CHUNKS - 1):
                    nc.vector.tensor_copy(centred[:], acc).then_inc(sum_ready, 1)
                else:
                    dve.wait_ge(side_saved, side_chunks(CHUNKS) if sweep == 1 else side_chunks(2 * CHUNKS))
                    nc.vector.tensor_tensor(centred[:], acc, part[:, chunk_cols(i)], ALU.add).then_inc(sum_ready, 1)

            def result(c):
                e = c - 2 * CHUNKS
                i = chunks[c][1]
                dve.wait_ge(h_ready, CHUNKS + e + 1)
                dve.wait_ge(x1_back[i % 2], 16 * (e // 2 + 1))
                nc.vector.tensor_tensor(h_buf[:], h_buf[:], x_buf[:, i % 2], ALU.add).then_inc(out_ready, 1)

            dve.wait_ge(consts_loaded, 16 * 6)
            for i in range(CHUNKS):
                dve.wait_ge(x_loaded[i % 2], 16 * (i // 2 + 1))
                centre(i, x_buf[:, i % 2])
                invert(i)
                norm(i)
                save_g(i, 0, i)
                dve.wait_ge(self_product, i + 1)
                nc.vector.scalar_tensor_tensor(out=g_all[:, 1, chunk_cols(i)], in0=work_ps[:],
                                               scalar=biases[:, 0:1], in1=x_buf[:, i % 2],
                                               op0=ALU.add, op1=ALU.add).then_inc(base_saved, 1)
            for c in range(len(chunks)):
                sweep = chunks[c][0]
                hooks = {}
                if 1 <= c < CHUNKS:
                    l, src = CHUNKS + c - 1, x_buf[:, (c - 1) % 2]
                    hooks = {3: lambda: finish_sum(c - 1), 6: lambda: centre(l, src), 12: lambda: invert(l),
                             13: lambda: norm(l), 15: lambda: save_g(l, 1, c - 1)}
                elif CHUNKS < c <= 2 * CHUNKS:
                    hooks = {3: lambda: finish_sum(c - 1), 7: lambda: save_g(CHUNKS + c - 1, 0, chunks[c - 1][1])}
                elif c > 2 * CHUNKS:
                    hooks = {3: lambda: finish_sum(c - 1), 6: lambda: result(c - 1)}
                if c == CHUNKS:
                    l, src = 2 * CHUNKS - 1, x_buf[:, (CHUNKS - 1) % 2]
                    finish_sum(c - 1)
                    centre(l, src)
                    invert(l)
                    norm(l)
                    save_g(l, 1, CHUNKS - 1)
                run_chunk(dve, c, lambda j, n, shared, g_needed, hook: split_block(sweep, j, n, shared, hook), hooks)
            finish_sum(len(chunks) - 1)
            result(len(chunks) - 1)

        @block.tensor
        def _(pe):
            def over_partitions(source, done):
                for half in range(HALVES):
                    mm = nc.tensor.matmul(work_ps[:, cols(half)], mean_w[:], source[:, cols(half)],
                                          start=True, stop=True)
                mm.then_inc(done, 1)

            def mean(l, source):
                over_partitions(source, mean_ready)

            def variance(l):
                pe.wait_ge(squares_ready, l + 1)
                over_partitions(spread, var_ready)

            def make_g(weights):
                for s in range(SLABS):
                    mm = nc.tensor.matmul(work_ps[:, s * F:(s + 1) * F], h_buf[:, s * P:(s + 1) * P], weights,
                                          start=True, stop=True)
                mm.then_inc(g_product, 1)

            def open_acc(acc):
                for half in range(HALVES):
                    nc.tensor.matmul(acc[:, half * BANK:half * BANK + 2], zeros[:], zeros[:, 0:2],
                                     start=True, stop=False, skip_group_check=True)

            def product_block(c, n, shared, hook):
                sweep = chunks[c][0]
                accs = [(LEAD[sweep], lead_acc[:, c % 2])]
                if shared:
                    accs.append((SIDE[sweep], side_acc[:]))
                for u in range(SLABS):
                    pe.wait_ge(rest_ready, n * SLABS + (u + 1))
                    for g, acc in accs:
                        for w, a in ((g_high, a_high), (g_high, a_rest), (g_rest, a_high)):
                            for half in range(HALVES):
                                mm = nc.tensor.matmul(acc[:, cols(half)], w[:, g, u], a[:, u % DEPTH, cols(half)],
                                                      start=False, stop=False, skip_group_check=True)
                    mm.then_inc(slab_used, 1)
                    if u in hook:
                        hook[u]()

            pe.wait_ge(consts_set, 1)
            pe.wait_ge(consts_loaded, 16 * 6)
            for i in range(CHUNKS):
                pe.wait_ge(x_loaded[i % 2], 16 * (i // 2 + 1))
                if i:
                    pe.wait_ge(base_saved, i)
                mean(i, x_buf[:, i % 2])
                variance(i)
                pe.wait_ge(normed, i + 1)
                make_g(w0_sb[:, 1])
                pe.wait_ge(g_saved, i + 1)
                for half in range(HALVES):
                    mm = nc.tensor.matmul(work_ps[:, cols(half)], w0_sb[:, 0], h_buf[:, cols(half)],
                                          start=True, stop=True)
                mm.then_inc(self_product, 1)

            def next_mean(c):
                pe.wait_ge(sum_ready, c + 1)
                if c == 0:
                    pe.wait_ge(base_saved, CHUNKS)
                else:
                    pe.wait_ge(g_saved, CHUNKS + c)
                mean(CHUNKS + c, x_buf[:, c % 2])

            def g1(c):
                pe.wait_ge(normed, CHUNKS + c + 1)
                make_g(w1_sb[:])

            def g2(c):
                pe.wait_ge(h_ready, c - CHUNKS + 1)
                pe.wait_ge(g_saved, CHUNKS + c)
                make_g(w2_sb[:])

            def open_side(c):
                if side_chunks(c):
                    pe.wait_ge(side_saved, side_chunks(c))
                open_acc(side_acc[:])

            for c in range(len(chunks)):
                hooks = {}
                if 1 <= c < CHUNKS:
                    hooks = {2: lambda: next_mean(c - 1), 5: lambda: variance(CHUNKS + c - 1), 11: lambda: g1(c - 1)}
                elif CHUNKS < c <= 2 * CHUNKS:
                    hooks = {3: lambda: g2(c - 1)}
                if c == CHUNKS:
                    next_mean(c - 1)
                    variance(2 * CHUNKS - 1)
                    g1(c - 1)
                if c >= 2:
                    pe.wait_ge(sum_ready, c - 1)
                open_acc(lead_acc[:, c % 2])
                run_chunk(pe, c, lambda j, n, shared, g_needed, hook: product_block(c, n, shared, hook), hooks,
                          at_side=lambda: open_side(c))


def kernel(x, adj, L0_gnn_W, L0_gnn_b, L1_gnn_W1, L1_gnn_b1, L1_gnn_W2, L1_gnn_b2):
    import numpy as np
    import concourse.bacc as bacc
    from concourse.bass_utils import run_bass_kernel_spmd

    adj_t = np.asarray(adj).reshape(CHUNKS, R, N // (P * PER_TILE), PER_TILE, P).transpose(0, 2, 4, 3, 1)
    arrays = {
        "adj_t": adj_t,
        "x_t": np.asarray(x).reshape(CHUNKS, R, F).transpose(0, 2, 1),
        "w0_t": np.asarray(L0_gnn_W).T,
        "b0": np.asarray(L0_gnn_b).reshape(F, 1),
        "w1": np.asarray(L1_gnn_W1),
        "b1": np.asarray(L1_gnn_b1).reshape(F, 1),
        "w2": np.asarray(L1_gnn_W2),
        "b2": np.asarray(L1_gnn_b2).reshape(F, 1),
    }
    arrays = {k: np.ascontiguousarray(v) for k, v in arrays.items()}

    nc = bacc.Bacc("TRN2", target_bir_lowering=False, num_devices=1)
    ins = [nc.dram_tensor(f"in_{k}", v.shape, mybir.dt.from_np(v.dtype), kind="ExternalInput").ap()
           for k, v in arrays.items()]
    out_t = nc.dram_tensor("out_t", [CHUNKS, F, R], F32, kind="ExternalOutput").ap()
    build(nc, *ins, out_t)
    r = run_bass_kernel_spmd(nc, [{f"in_{k}": v for k, v in arrays.items()}], core_ids=[0])
    return np.ascontiguousarray(r.results[0]["out_t"].transpose(0, 2, 1)).reshape(N, F)
```

```python
from contextlib import ExitStack

import concourse.bass as bass
from concourse import mybir

F32 = mybir.dt.float32
F32R = mybir.dt.float32r
BF16 = mybir.dt.bfloat16
ALU = mybir.AluOpType
ACT = mybir.ActivationFunctionType

P = 128
N = 8192
F = 128
R = 1024
CHUNKS = N // R
BANK = 512
HALVES = R // BANK
SLABS = R // P
PER_TILE = 2
TILES = SLABS // PER_TILE
DEPTH = 4
HALF = SLABS // 2
EPS = 1e-5


def plan():
    chunks = []
    for i in range(CHUNKS):
        lead, side = (i, 1, False), (0, 1, True)
        if i <= 1:
            runs = [(CHUNKS - i, [lead]), (i, [side])]
        else:
            pairs = min(CHUNKS - i, i)
            runs = [(pairs, [lead, side]), (CHUNKS - i - pairs, [(i + pairs, 1, False)]),
                    (i - pairs, [(pairs, 1, True)])]
        chunks.append((0, i, runs))
    for i in reversed(range(CHUNKS)):
        chunks.append((1, i, [(1, [(i, 1, False)]), (CHUNKS - 1 - i, [(CHUNKS - 1, -1, True)])]))
    for i in reversed(range(CHUNKS)):
        chunks.append((2, i, [(i + 1, [(i, -1, False)])]))
    return [(sweep, i, [run for run in runs if run[0]]) for sweep, i, runs in chunks]


def has_side(runs):
    return any(shared for _, blocks in runs for _, _, shared in blocks)


LEAD = (0, 1, 0)
SIDE = (1, 0, None)


def g_count(sweep, j, of_side):
    which = sweep + (1 if of_side else 0)
    if which == 0:
        return 1 + j
    if which == 1:
        return CHUNKS + 1 + j
    return 3 * CHUNKS - j


def build(nc, adj_t, x_rows, x_t, w0_t, b0, w1, b1, w2, b2, out_t):
    chunks = plan()
    starts = [0]
    for _, _, runs in chunks:
        starts.append(starts[-1] + sum(count * len(blocks) for count, blocks in runs))

    with ExitStack() as ctx:
        def sb(name, shape, dt=F32):
            return ctx.enter_context(nc.sbuf_tensor(name, shape, dt))

        def psum(name, shape):
            return ctx.enter_context(nc.psum_tensor(name, shape, F32))

        def sem(name):
            return ctx.enter_context(nc.semaphore(name))

        x1_dram = nc.dram_tensor("x1_t", [CHUNKS, F, R], F32, kind="Internal").ap()

        lead_acc = psum("lead_acc", [P, 2, R])
        side_acc = psum("side_acc", [P, R])
        work_ps = psum("work_ps", [P, R])

        g_all = sb("g_all", [P, 2, N])
        part = sb("part", [P, N])
        a_ring = sb("a_ring", [P, TILES, PER_TILE, R])
        a_high = sb("a_high", [P, DEPTH, R], F32R)
        a_rest = sb("a_rest", [P, DEPTH, R], F32R)
        g_high = sb("g_high", [P, 2, SLABS, F], F32R)
        g_rest = sb("g_rest", [P, 2, SLABS, F], F32R)
        x_buf = sb("x_buf", [P, 2, R])
        total = sb("total", [P, R])
        squares = sb("squares", [P, R])
        h_buf = sb("h_buf", [P, R])
        h_bufs = (h_buf, squares)
        x_norm = part
        base = g_all[:, 1]
        stats = sb("stats", [P, SLABS, 6])
        mean_var = sb("mean_var", [P, 2, SLABS, 2])
        dev = sb("dev", [P, 2, SLABS])
        inv = sb("inv", [P, SLABS])
        shift = sb("shift", [P, SLABS])
        w0_sb = sb("w0_sb", [P, 2, F])
        w1_sb = sb("w1_sb", [P, F])
        w2_sb = sb("w2_sb", [P, F])
        biases = sb("biases", [P, 3])
        eps_col = sb("eps_col", [P, 1])
        mean_col = sb("mean_col", [P, 1])
        centring = sb("centring", [P, F])
        table_ready = sb("table_ready", [P, 1])
        identity = sb("identity", [P, P])
        zeros = sb("zeros", [P, P], BF16)

        consts_loaded = sem("consts_loaded")
        consts_set = sem("consts_set")
        diagonals = sem("diagonals")
        tile_loaded = [sem(f"tile_loaded{v}") for v in range(TILES)]
        high_ready = sem("high_ready")
        rest_ready = sem("rest_ready")
        slab_used = sem("slab_used")
        rows_loaded = [sem(f"rows_loaded{i}") for i in range(CHUNKS)]
        x_t_loaded = [sem(f"x_t_loaded{i}") for i in range(CHUNKS)]
        x1_stored = [sem(f"x1_stored{p}") for p in range(2)]
        x1_back = [sem(f"x1_back{p}") for p in range(2)]
        stats_ready = sem("stats_ready")
        var_ready = sem("var_ready")
        dev_ready = sem("dev_ready")
        inv_ready = sem("inv_ready")
        shift_ready = sem("shift_ready")
        rows_normed = sem("rows_normed")
        turned = sem("turned")
        h0_ready = sem("h0_ready")
        centred = sem("centred")
        squares_ready = sem("squares_ready")
        x1_var_ready = sem("x1_var_ready")
        g_product = sem("g_product")
        g_saved = sem("g_saved")
        self_product = sem("self_product")
        base_saved = sem("base_saved")
        sum_ready = sem("sum_ready")
        side_saved = sem("side_saved")
        h_ready = sem("h_ready")
        out_ready = sem("out_ready")
        out_stored = sem("out_stored")

        block = ctx.enter_context(nc.Block())

        def cols(half):
            return slice(half * BANK, (half + 1) * BANK)

        turned_ps, g0_ps, self_ps = work_ps[:], side_acc, lead_acc[:, 1]

        def spread_prologue(steps):
            return {b * SLABS + k: [(step, b + ahead) for step, ahead in todo if b + ahead < CHUNKS]
                    for b in range(CHUNKS) for k, todo in steps.items()}

        def chunk_cols(i):
            return slice(i * R, (i + 1) * R)

        def side_chunks(c):
            return sum(1 for _, _, runs in chunks[:c] if has_side(runs))

        def run_chunk(eng, c, one_block, hooks=None, at_side=None):
            sweep, _, runs = chunks[c]
            hooks = hooks or {}
            n_peeled = max(1 + max(hooks, default=-1) // SLABS, c == 0)
            n, done, side_open = starts[c], 0, False
            for count, blocks in runs:
                t = 0
                while t < count and (done < n_peeled or count - t == 1):
                    for j0, dj, shared in blocks:
                        if shared and at_side and not side_open:
                            at_side()
                            side_open = True
                        one_block(j0 + dj * t, n, shared, g_count(sweep, j0, shared) + t,
                                  {k - done * SLABS: f for k, f in hooks.items()
                                   if done * SLABS <= k < (done + 1) * SLABS})
                        n, done = n + 1, done + 1
                    t += 1
                if t == count:
                    continue
                if at_side and not side_open and any(shared for _, _, shared in blocks):
                    at_side()
                    side_open = True
                with eng.Fori(0, count - t) as k:
                    for q, (j0, dj, shared) in enumerate(blocks):
                        j = k + (j0 + t) if dj > 0 else k * -1 + (j0 - t)
                        one_block(j, k * len(blocks) + (n + q), shared, k + (g_count(sweep, j0, shared) + t), {})
                n += (count - t) * len(blocks)

        @block.sync
        def _(sp):
            def load_block(i, j, n):
                for v in range(TILES):
                    if not (isinstance(n, int) and n == 0):
                        sp.wait_ge(rest_ready, n * SLABS + (PER_TILE * (v + 1) - SLABS))
                    sp.dma_start(a_ring[:, v], adj_t[i, bass.ds(j * TILES + v, 1)].rearrange(
                        "o p s r -> p (o s) r")).then_inc(tile_loaded[v], 16)

            for i in range(3):
                sp.dma_start(x_norm[:, chunk_cols(i)], x_rows[i]).then_inc(rows_loaded[i], 16)
            sp.dma_start(w0_sb[:], w0_t.rearrange("(s p) f -> p s f", p=P)).then_inc(consts_loaded, 16)
            sp.dma_start(w1_sb[:], w1).then_inc(consts_loaded, 16)
            sp.dma_start(w2_sb[:], w2).then_inc(consts_loaded, 16)
            for q, b in enumerate((b0, b1, b2)):
                sp.dma_start(biases[:, q:q + 1], b).then_inc(consts_loaded, 16)
            sp.dma_start(base[:, chunk_cols(0)], x_t[0]).then_inc(x_t_loaded[0], 16)
            for c in range(len(chunks)):
                i = chunks[c][1]
                run_chunk(sp, c, lambda j, n, shared, g_needed, hook: load_block(i, j, n))

        @block.gpsimd
        def _(pool):
            nc.gpsimd.memset(identity[:], 0.0).then_inc(diagonals, 1)
            nc.gpsimd.memset(centring[:], -1.0 / F).then_inc(diagonals, 1)
            pool.wait_ge(diagonals, 2)
            for square, on_diagonal in ((identity, 1.0), (centring, 1.0 - 1.0 / F)):
                nc.gpsimd.affine_select(out=square[:], in_=square[:], compare_op=ALU.not_equal, fill=on_diagonal,
                                        base=0, pattern=[[-1, P]], channel_multiplier=1)
            nc.gpsimd.memset(mean_col[:], 1.0 / F)
            nc.gpsimd.memset(eps_col[:], EPS)
            nc.gpsimd.memset(zeros[:], 0.0).then_inc(consts_set, 1)
            for i in range(1, CHUNKS):
                if i >= 3:
                    pool.dma_start(x_norm[:, chunk_cols(i)], x_rows[i]).then_inc(rows_loaded[i], 16)
                pool.dma_start(base[:, chunk_cols(i)], x_t[i]).then_inc(x_t_loaded[i], 16)
            for i in range(CHUNKS):
                pool.wait_ge(sum_ready, i + 1)
                pool.dma_start(x1_dram[i], x_buf[:, i % 2]).then_inc(x1_stored[i % 2], 16)
            for p in range(2):
                pool.wait_ge(x1_stored[p], 16 * (CHUNKS // 2))
            for e, i in enumerate(reversed(range(CHUNKS))):
                if e < 2:
                    pool.wait_ge(centred, CHUNKS)
                else:
                    pool.wait_ge(out_ready, e - 1)
                pool.dma_start(x_buf[:, i % 2], x1_dram[i]).then_inc(x1_back[i % 2], 16)
                if e >= 1:
                    pool.wait_ge(out_ready, e)
                    pool.dma_start(out_t[i + 1], h_buf[:]).then_inc(out_stored, 16)
            pool.wait_ge(out_ready, CHUNKS)
            pool.dma_start(out_t[0], h_buf[:]).then_inc(out_stored, 16)
            pool.wait_ge(out_stored, 16 * CHUNKS)

        @block.scalar
        def _(act):
            def deviation(k, variances):
                nc.scalar.activation(dev[:, k % 2], variances, ACT.Sqrt, bias=eps_col[:, 0:1]).then_inc(dev_ready, 1)

            def row_deviation(i):
                act.wait_ge(var_ready, i + 1)
                deviation(i, mean_var[:, i % 2, :, 1])

            def norm_rows(i, slabs):
                act.wait_ge(shift_ready, i + 1)
                for s in slabs:
                    rows = x_norm[:, i * R + s * F:i * R + (s + 1) * F]
                    a = nc.scalar.activation(rows, rows, ACT.Relu, bias=shift[:, s:s + 1], scale=inv[:, s:s + 1])
                if s == SLABS - 1:
                    a.then_inc(rows_normed, 1)

            def norm_first_rows(i):
                norm_rows(i, range(HALF))

            def norm_last_rows(i):
                norm_rows(i, range(HALF, SLABS))

            def save_h0(i):
                act.wait_ge(turned, i + 1)
                if i >= 2:
                    act.wait_ge(self_product, i - 1)
                nc.scalar.activation(h_bufs[i % 2][:], turned_ps, ACT.Copy).then_inc(h0_ready, 1)

            def save_g0(i):
                act.wait_ge(g_product, i + 1)
                nc.scalar.activation(g_all[:, 0, chunk_cols(i)], g0_ps[:], ACT.Copy).then_inc(g_saved, 1)

            def relu_and_squares(c):
                act.wait_ge(centred, c + 1)
                nc.scalar.activation(h_buf[:], work_ps[:], ACT.Relu)
                nc.scalar.activation(squares[:], work_ps[:], ACT.Square).then_inc(squares_ready, 1)

            def x1_deviation(c):
                act.wait_ge(x1_var_ready, c + 1)
                deviation(CHUNKS + c, work_ps[:, 0:SLABS])

            def split_block(sweep, j, n, shared, g_needed, hook):
                for u in range(SLABS):
                    if u % PER_TILE == 0:
                        act.wait_ge(tile_loaded[u // PER_TILE], n * 16 + 16)
                    if not (isinstance(n, int) and n == 0) or u >= DEPTH:
                        act.wait_ge(slab_used, n * SLABS + (u + 1 - DEPTH))
                    if u % HALF == 0:
                        a, b = (0, 2) if shared else (LEAD[sweep], LEAD[sweep] + 1)
                        if u == 0:
                            act.wait_ge(g_saved, g_needed)
                        nc.scalar.activation(
                            g_high[:, a:b, u:u + HALF].rearrange("p g s f -> p g (s f)"),
                            g_all[:, a:b, bass.ds(j * R + u * F, HALF * F)], ACT.Copy)
                    nc.scalar.activation(a_high[:, u % DEPTH], a_ring[:, u // PER_TILE, u % PER_TILE],
                                         ACT.Copy).then_inc(high_ready, 1)
                    for step, chunk in hook.get(u, ()):
                        step(chunk)

            def save_side(c):
                sweep, i, runs = chunks[c]
                if has_side(runs):
                    act.wait_ge(slab_used, SLABS * starts[c + 1])
                    if sweep == 1:
                        act.wait_ge(sum_ready, c + 1)
                    nc.scalar.activation(part[:, chunk_cols(i)], side_acc[:], ACT.Copy).then_inc(side_saved, 1)

            def relu(c):
                act.wait_ge(sum_ready, c + 1)
                e = c - 2 * CHUNKS
                if e >= 1:
                    act.wait_ge(out_stored, 16 * e)
                q = chunks[c][0]
                nc.scalar.activation(h_buf[:], total[:], ACT.Relu, bias=biases[:, q:q + 1]).then_inc(h_ready, 1)

            act.wait_ge(consts_set, 1)
            nc.scalar.activation(table_ready[:], eps_col[:], ACT.Sqrt)
            row_deviation(0)
            norm_first_rows(0)
            norm_last_rows(0)
            row_deviation(1)
            norm_first_rows(1)
            norm_last_rows(1)
            save_h0(0)
            row_deviation(2)
            save_g0(0)
            save_h0(1)
            norm_first_rows(2)
            norm_last_rows(2)
            for c in range(len(chunks)):
                sweep = chunks[c][0]
                hooks = {}
                if c == 0:
                    hooks = spread_prologue({2: [(row_deviation, 3)], 3: [(save_g0, 1)],
                                             5: [(norm_first_rows, 3), (save_h0, 2)], 7: [(norm_last_rows, 3)]})
                if c == 1:
                    act.wait_ge(consts_loaded, 16 * 6)
                if 1 <= c < CHUNKS:
                    hooks = {5: [(save_side, c - 1)], 7: [(relu_and_squares, c - 1)], 12: [(x1_deviation, c - 1)]}
                elif c > CHUNKS:
                    hooks = {4: [(relu, c - 1)], 5: [(save_side, c - 1)]}
                if c == CHUNKS:
                    save_side(c - 1)
                    relu_and_squares(c - 1)
                    x1_deviation(c - 1)
                run_chunk(act, c, lambda j, n, shared, g_needed, hook: split_block(
                    sweep, j, n, shared, g_needed, hook), hooks)
            relu(len(chunks) - 1)

        @block.vector
        def _(dve):
            def row_stats(i):
                dve.wait_ge(rows_loaded[i], 16)
                if i:
                    dve.wait_ge(var_ready, i)
                for s in range(SLABS):
                    bn = nc.vector.bn_stats(stats[:, s], x_norm[:, i * R + s * F:i * R + (s + 1) * F])
                bn.then_inc(stats_ready, 1)
                dve.wait_ge(stats_ready, i + 1)
                if i >= 2:
                    dve.wait_ge(dev_ready, i - 1)
                for s in range(SLABS):
                    bn = nc.vector.bn_aggr(mean_var[:, i % 2, s], stats[:, s])
                bn.then_inc(var_ready, 1)

            def invert(k):
                dve.wait_ge(dev_ready, k + 1)
                nc.vector.reciprocal(inv[:], dev[:, k % 2]).then_inc(inv_ready, 1)
                dve.wait_ge(inv_ready, k + 1)

            def row_shift(i):
                if i:
                    dve.wait_ge(rows_normed, i)
                invert(i)
                nc.vector.scalar_tensor_tensor(out=shift[:], in0=mean_var[:, i % 2, :, 0], scalar=-1.0, in1=inv[:],
                                               op0=ALU.mult, op1=ALU.mult).then_inc(shift_ready, 1)

            def add_base(i):
                dve.wait_ge(x_t_loaded[i], 16)
                dve.wait_ge(self_product, i + 1)
                nc.vector.scalar_tensor_tensor(out=base[:, chunk_cols(i)], in0=self_ps,
                                               scalar=biases[:, 0:1], in1=base[:, chunk_cols(i)],
                                               op0=ALU.add, op1=ALU.add).then_inc(base_saved, 1)

            def save_g1(c):
                invert(CHUNKS + c)
                dve.wait_ge(g_product, CHUNKS + c + 1)
                nc.vector.tensor_tensor(
                    g_all[:, 1, chunk_cols(c)].rearrange("p (s f) -> p s f", f=F),
                    work_ps[:].rearrange("p (s f) -> p s f", f=F),
                    inv[:].unsqueeze(2).to_broadcast([P, SLABS, F]), ALU.mult).then_inc(g_saved, 1)

            def save_g2(c):
                dve.wait_ge(g_product, CHUNKS + c + 1)
                nc.vector.tensor_copy(g_all[:, 0, chunk_cols(chunks[c][1])], work_ps[:]).then_inc(g_saved, 1)

            def split_block(sweep, j, n, shared, hook):
                for u in range(SLABS):
                    dve.wait_ge(high_ready, n * SLABS + (u + 1))
                    if u % HALF == 0:
                        a, b = (0, 2) if shared else (LEAD[sweep], LEAD[sweep] + 1)
                        nc.vector.tensor_tensor(
                            g_rest[:, a:b, u:u + HALF].rearrange("p g s f -> p g (s f)"),
                            g_all[:, a:b, bass.ds(j * R + u * F, HALF * F)],
                            g_high[:, a:b, u:u + HALF].rearrange("p g s f -> p g (s f)").bitcast(F32),
                            ALU.subtract)
                    nc.vector.tensor_tensor(a_rest[:, u % DEPTH], a_ring[:, u // PER_TILE, u % PER_TILE],
                                            a_high[:, u % DEPTH].bitcast(F32), ALU.subtract).then_inc(rest_ready, 1)
                    for step, chunk in hook.get(u, ()):
                        step(chunk)

            def finish_sum(c):
                sweep, i, _ = chunks[c]
                dve.wait_ge(slab_used, SLABS * starts[c + 1])
                acc = lead_acc[:, c % 2]
                if sweep == 0:
                    dve.wait_ge(base_saved, CHUNKS)
                    if i >= 2:
                        dve.wait_ge(x1_stored[i % 2], 16 * (i // 2))
                    nc.vector.tensor_tensor(x_buf[:, i % 2], acc, base[:, chunk_cols(i)], ALU.add
                                            ).then_inc(sum_ready, 1)
                elif (sweep == 1 and i == 0) or (sweep == 2 and i == CHUNKS - 1):
                    nc.vector.tensor_copy(total[:], acc).then_inc(sum_ready, 1)
                else:
                    dve.wait_ge(side_saved, side_chunks(CHUNKS) if sweep == 1 else side_chunks(2 * CHUNKS))
                    nc.vector.tensor_tensor(total[:], acc, part[:, chunk_cols(i)], ALU.add).then_inc(sum_ready, 1)

            def result(c):
                e = c - 2 * CHUNKS
                i = chunks[c][1]
                dve.wait_ge(h_ready, CHUNKS + e + 1)
                dve.wait_ge(x1_back[i % 2], 16 * (e // 2 + 1))
                nc.vector.tensor_tensor(h_buf[:], h_buf[:], x_buf[:, i % 2], ALU.add).then_inc(out_ready, 1)

            for i in range(3):
                row_stats(i)
                row_shift(i)
            dve.wait_ge(consts_loaded, 16 * 6)
            add_base(0)
            for c in range(len(chunks)):
                sweep = chunks[c][0]
                hooks = {}
                if c == 0:
                    hooks = spread_prologue({0: [(row_stats, 3)], 4: [(row_shift, 3)], 5: [(add_base, 1)]})
                if 1 <= c < CHUNKS:
                    hooks = {3: [(finish_sum, c - 1)], 15: [(save_g1, c - 1)]}
                elif CHUNKS < c <= 2 * CHUNKS:
                    hooks = {3: [(finish_sum, c - 1)], 7: [(save_g2, c - 1)]}
                elif c > 2 * CHUNKS:
                    hooks = {3: [(finish_sum, c - 1)], 6: [(result, c - 1)]}
                if c == CHUNKS:
                    finish_sum(c - 1)
                    save_g1(c - 1)
                run_chunk(dve, c, lambda j, n, shared, g_needed, hook: split_block(sweep, j, n, shared, hook), hooks)
            finish_sum(len(chunks) - 1)
            result(len(chunks) - 1)

        @block.tensor
        def _(pe):
            def turn(i):
                pe.wait_ge(rows_normed, i + 1)
                if i:
                    pe.wait_ge(h0_ready, i)
                for s in range(SLABS):
                    mm = nc.tensor.transpose(turned_ps[:, s * P:(s + 1) * P],
                                             x_norm[:, i * R + s * F:i * R + (s + 1) * F], identity[:])
                mm.then_inc(turned, 1)

            def g0(i):
                pe.wait_ge(h0_ready, i + 1)
                if i:
                    pe.wait_ge(g_saved, i)
                make_g(g0_ps, h_bufs[i % 2], w0_sb[:, 1])

            def self_term(i):
                if i:
                    pe.wait_ge(base_saved, i)
                for half in range(HALVES):
                    mm = nc.tensor.matmul(self_ps[:, cols(half)], w0_sb[:, 0], h_bufs[i % 2][:, cols(half)],
                                          start=True, stop=True)
                mm.then_inc(self_product, 1)

            def centre(c):
                pe.wait_ge(sum_ready, c + 1)
                pe.wait_ge(g_saved, CHUNKS + c)
                for half in range(HALVES):
                    mm = nc.tensor.matmul(work_ps[:, cols(half)], centring[:], x_buf[:, c % 2, cols(half)],
                                          start=True, stop=True)
                mm.then_inc(centred, 1)

            def x1_variance(c):
                pe.wait_ge(squares_ready, c + 1)
                for s in range(SLABS):
                    mm = nc.tensor.matmul(work_ps[:, s:s + 1], squares[:, s * P:(s + 1) * P], mean_col[:],
                                          start=True, stop=True)
                mm.then_inc(x1_var_ready, 1)

            def make_g(out, h, weights):
                for s in range(SLABS):
                    mm = nc.tensor.matmul(out[:, s * F:(s + 1) * F], h[:, s * P:(s + 1) * P], weights,
                                          start=True, stop=True)
                mm.then_inc(g_product, 1)

            def open_acc(acc):
                for half in range(HALVES):
                    nc.tensor.matmul(acc[:, half * BANK:half * BANK + 2], zeros[:], zeros[:, 0:2],
                                     start=True, stop=False, skip_group_check=True)

            def product_block(c, n, shared, hook):
                sweep = chunks[c][0]
                accs = [(LEAD[sweep], lead_acc[:, c % 2])]
                if shared:
                    accs.append((SIDE[sweep], side_acc[:]))
                for u in range(SLABS):
                    pe.wait_ge(rest_ready, n * SLABS + (u + 1))
                    for g, acc in accs:
                        for w, a in ((g_high, a_high), (g_high, a_rest), (g_rest, a_high)):
                            for half in range(HALVES):
                                mm = nc.tensor.matmul(acc[:, cols(half)], w[:, g, u], a[:, u % DEPTH, cols(half)],
                                                      start=False, stop=False, skip_group_check=True)
                    mm.then_inc(slab_used, 1)
                    for step, chunk in hook.get(u, ()):
                        step(chunk)

            pe.wait_ge(consts_set, 1)
            turn(0)
            pe.wait_ge(consts_loaded, 16 * 6)
            g0(0)
            self_term(0)
            turn(1)
            g0(1)

            def g1(c):
                pe.wait_ge(dev_ready, CHUNKS + c + 1)
                make_g(work_ps, h_buf, w1_sb[:])

            def g2(c):
                pe.wait_ge(h_ready, c - CHUNKS + 1)
                pe.wait_ge(g_saved, CHUNKS + c)
                make_g(work_ps, h_buf, w2_sb[:])

            def open_side(c):
                if side_chunks(c):
                    pe.wait_ge(side_saved, side_chunks(c))
                open_acc(side_acc[:])

            for c in range(len(chunks)):
                hooks = {}
                if c == 0:
                    hooks = spread_prologue({0: [(turn, 2)], 1: [(self_term, 1)], 6: [(g0, 2)]})
                if c == 1:
                    pe.wait_ge(h0_ready, CHUNKS)
                    pe.wait_ge(g_saved, CHUNKS)
                    pe.wait_ge(base_saved, CHUNKS)
                if 1 <= c < CHUNKS:
                    hooks = {2: [(centre, c - 1)], 7: [(x1_variance, c - 1)], 11: [(g1, c - 1)]}
                elif CHUNKS < c <= 2 * CHUNKS:
                    hooks = {3: [(g2, c - 1)]}
                if c == CHUNKS:
                    centre(c - 1)
                    x1_variance(c - 1)
                    g1(c - 1)
                if c >= 2:
                    pe.wait_ge(sum_ready, c - 1)
                open_acc(lead_acc[:, c % 2])
                run_chunk(pe, c, lambda j, n, shared, g_needed, hook: product_block(c, n, shared, hook), hooks,
                          at_side=lambda: open_side(c))


def kernel(x, adj, L0_gnn_W, L0_gnn_b, L1_gnn_W1, L1_gnn_b1, L1_gnn_W2, L1_gnn_b2):
    import numpy as np
    import concourse.bacc as bacc
    from concourse.bass_utils import run_bass_kernel_spmd

    adj_t = np.asarray(adj).reshape(CHUNKS, R, N // (P * PER_TILE), PER_TILE, P).transpose(0, 2, 4, 3, 1)
    arrays = {
        "adj_t": adj_t,
        "x_rows": np.asarray(x).reshape(CHUNKS, SLABS, P, F).transpose(0, 2, 1, 3).reshape(CHUNKS, P, R),
        "x_t": np.asarray(x).reshape(CHUNKS, R, F).transpose(0, 2, 1),
        "w0_t": np.asarray(L0_gnn_W).T,
        "b0": np.asarray(L0_gnn_b).reshape(F, 1),
        "w1": np.asarray(L1_gnn_W1),
        "b1": np.asarray(L1_gnn_b1).reshape(F, 1),
        "w2": np.asarray(L1_gnn_W2),
        "b2": np.asarray(L1_gnn_b2).reshape(F, 1),
    }
    arrays = {k: np.ascontiguousarray(v) for k, v in arrays.items()}

    nc = bacc.Bacc("TRN2", target_bir_lowering=False, num_devices=1)
    ins = [nc.dram_tensor(f"in_{k}", v.shape, mybir.dt.from_np(v.dtype), kind="ExternalInput").ap()
           for k, v in arrays.items()]
    out_t = nc.dram_tensor("out_t", [CHUNKS, F, R], F32, kind="ExternalOutput").ap()
    build(nc, *ins, out_t)
    r = run_bass_kernel_spmd(nc, [{f"in_{k}": v for k, v in arrays.items()}], core_ids=[0])
    return np.ascontiguousarray(r.results[0]["out_t"].transpose(0, 2, 1)).reshape(N, F)
```

```python
from collections import namedtuple
from contextlib import ExitStack

import concourse.bass as bass
from concourse import mybir

F32 = mybir.dt.float32
F32R = mybir.dt.float32r
BF16 = mybir.dt.bfloat16
ALU = mybir.AluOpType
ACT = mybir.ActivationFunctionType

P = 128
N = 8192
F = 128
R = 1024
CHUNKS = N // R
BANK = 512
HALVES = R // BANK
SLABS = R // P
PER_TILE = 2
TILES = SLABS // PER_TILE
DEPTH = 4
TILES_OF_ROWS = CHUNKS * TILES
HALF = SLABS // 2
EPS = 1e-5

LEAD_ONLY, SHARED, SIDE_ONLY, EXTRA = "lead", "shared", "side", "extra"

Block = namedtuple("Block", "chunk rows j n kind g_needed extras extra_rows slab")

LEAD = (0, 1, 0)
SIDE = (1, 0)

LATE = 2

EARLY = 2 * CHUNKS + CHUNKS // 2
FETCHED = CHUNKS - 2


def plan():
    chunks = []
    for i in range(CHUNKS):
        lead, side = (i, 0, i, 1, LEAD_ONLY), (i, 0, 0, 1, SHARED)
        if i == 0:
            runs = [(CHUNKS, [lead])]
        elif i <= 2:
            first = 3 if i == 1 else 1
            rest = CHUNKS // 2 + first + 1
            runs = [(first, [lead]), (1, [side]), (rest - i - first, [(i, 0, i + first, 1, LEAD_ONLY)]),
                    (i - 1, [(i, 0, 1, 1, SHARED)]), (CHUNKS - rest, [(i, 0, rest, 1, LEAD_ONLY)])]
        elif i == CHUNKS - 1:
            runs = [(LATE + 1, [(i, 0, i - LATE, 1, LEAD_ONLY), side]),
                    (i - 2 * LATE - 1, [(i, 0, LATE + 1, 1, SHARED)]),
                    (LATE, [(i, 0, i - LATE, 1, SIDE_ONLY)])]
        else:
            pairs = min(CHUNKS - i, i)
            runs = [(pairs, [lead, side]), (CHUNKS - i - pairs, [(i, 0, i + pairs, 1, LEAD_ONLY)]),
                    (i - pairs, [(i, 0, pairs, 1, SHARED)])]
        chunks.append((0, i, runs))
    for i in reversed(range(CHUNKS)):
        n_shared = CHUNKS - 1 - i
        runs = [(1, [(i, 0, i, 1, LEAD_ONLY)]),
                (min(n_shared, 1), [(i, 0, CHUNKS - 1, -1, SHARED)]),
                (n_shared - 1, [(i + 1, 1, i + 1, 0, EXTRA), (i, 0, CHUNKS - 2, -1, SHARED)]),
                (min(n_shared, 1) if i else 0, [(CHUNKS - 1, 0, i + 1, 0, EXTRA)])]
        chunks.append((1, i, runs))
    for i in reversed(range(CHUNKS)):
        last = 1 if i == CHUNKS - 1 else 0
        chunks.append((2, i, [(last + 1, [(i, 0, last, -1, LEAD_ONLY)])]))
    return [(sweep, i, [run for run in runs if run[0] > 0]) for sweep, i, runs in chunks]


def has_side(runs):
    return any(blk[-1] == SHARED for _, blocks in runs for blk in blocks)


def places(blk, sweep):
    if blk.kind == SHARED:
        return 0, 2
    g = LEAD[sweep] if blk.kind == LEAD_ONLY else SIDE[sweep]
    return g, g + 1


def straight_blocks(c):
    return CHUNKS if c == 0 else 2 if c < 2 * CHUNKS else 1


def g_count(sweep, j, kind):
    which = sweep + (kind != LEAD_ONLY)
    if which == 0:
        return 1 + j
    if which == 1:
        return CHUNKS + 1 + j
    return 3 * CHUNKS - j


def build(nc, adj_t, x_rows, x_t, w0_t, b0, w1, b1, w2, b2, out_t):
    chunks = plan()
    starts = [0]
    for _, _, runs in chunks:
        starts.append(starts[-1] + sum(count * len(blocks) for count, blocks in runs))
    extras_before = [0]
    for _, _, runs in chunks:
        extras_before.append(extras_before[-1] + sum(count for count, blocks in runs for blk in blocks
                                                     if blk[-1] == EXTRA))

    def ends_with_extra(c):
        return chunks[c][2][-1][1][-1][-1] == EXTRA

    lead_ends = starts[1:]
    lead_ends[CHUNKS - 1] -= LATE
    for c in range(len(chunks)):
        if ends_with_extra(c):
            lead_ends[c] -= 1
    late_slab = SLABS * (lead_ends[CHUNKS - 1] - starts[CHUNKS - 1])

    first_shared = []
    for _, _, runs in chunks:
        kinds = [blk[-1] for count, blocks in runs for _ in range(count) for blk in blocks]
        first_shared.append(kinds.index(SHARED) * SLABS if SHARED in kinds else None)

    freed, n = [None] * CHUNKS, starts[2 * CHUNKS - 1]
    for count, blocks in chunks[2 * CHUNKS - 1][2]:
        for t in range(count):
            for _, _, j0, dj, kind in blocks:
                if kind != EXTRA:
                    freed[j0 + dj * t] = n
                n += 1

    with ExitStack() as ctx:
        def sb(name, shape, dt=F32):
            return ctx.enter_context(nc.sbuf_tensor(name, shape, dt))

        def psum(name, shape):
            return ctx.enter_context(nc.psum_tensor(name, shape, F32))

        def sem(name):
            return ctx.enter_context(nc.semaphore(name))

        x1_dram = nc.dram_tensor("x1_t", [CHUNKS, F, R], F32, kind="Internal").ap()

        lead_acc = psum("lead_acc", [P, 2, R])
        side_acc = psum("side_acc", [P, R])
        work_ps = psum("work_ps", [P, R])

        g_all = sb("g_all", [P, 2, N])
        part = sb("part", [P, N])
        a_ring = sb("a_ring", [P, TILES, PER_TILE, R])
        a_high = sb("a_high", [P, DEPTH, R], F32R)
        a_rest = sb("a_rest", [P, DEPTH, R], F32R)
        g_high = sb("g_high", [P, 2, SLABS, F], F32R)
        g_rest = sb("g_rest", [P, 2, SLABS, F], F32R)
        x_buf = sb("x_buf", [P, 2, R])
        total = sb("total", [P, R])
        squares = sb("squares", [P, R])
        h_buf = sb("h_buf", [P, R])
        h_bufs = (h_buf, squares)
        x_norm = part
        base = g_all[:, 1]
        stats = sb("stats", [P, SLABS, 6])
        mean_var = sb("mean_var", [P, 2, SLABS, 2])
        dev = sb("dev", [P, 2, SLABS])
        inv = sb("inv", [P, SLABS])
        shift = sb("shift", [P, SLABS])
        w0_sb = sb("w0_sb", [P, 2, F])
        w1_sb = sb("w1_sb", [P, F])
        w2_sb = sb("w2_sb", [P, F])
        biases = sb("biases", [P, 3])
        eps_col = sb("eps_col", [P, 1])
        mean_col = sb("mean_col", [P, 1])
        centring = sb("centring", [P, F])
        table_ready = sb("table_ready", [P, 1])
        identity = sb("identity", [P, P])
        zeros = sb("zeros", [P, P], BF16)

        consts_loaded = sem("consts_loaded")
        consts_set = sem("consts_set")
        diagonals = sem("diagonals")
        tile_loaded = [sem(f"tile_loaded{v}") for v in range(TILES)]
        high_ready = sem("high_ready")
        g_high_ready = sem("g_high_ready")
        rest_ready = sem("rest_ready")
        slab_used = sem("slab_used")
        rows_loaded = [sem(f"rows_loaded{i}") for i in range(CHUNKS)]
        x_t_loaded = [sem(f"x_t_loaded{i}") for i in range(CHUNKS)]
        x1_stored = [sem(f"x1_stored{p}") for p in range(2)]
        x1_back = [sem(f"x1_back{i}") for i in range(FETCHED)]
        early_loaded = [sem(f"early_loaded{v}") for v in range(TILES)]
        stats_ready = sem("stats_ready")
        var_ready = sem("var_ready")
        dev_ready = sem("dev_ready")
        inv_ready = sem("inv_ready")
        shift_ready = sem("shift_ready")
        rows_normed = sem("rows_normed")
        turned = sem("turned")
        h0_ready = sem("h0_ready")
        centred = sem("centred")
        squares_ready = sem("squares_ready")
        x1_var_ready = sem("x1_var_ready")
        g_product = sem("g_product")
        g_saved = sem("g_saved")
        self_product = sem("self_product")
        base_saved = sem("base_saved")
        sum_ready = sem("sum_ready")
        side_saved = sem("side_saved")
        extra_saved = sem("extra_saved")
        h_ready = sem("h_ready")
        out_ready = sem("out_ready")
        last_out_ready = sem("last_out_ready")
        out_stored = [sem(f"out_stored{p}") for p in range(2)]

        block = ctx.enter_context(nc.Block())

        def cols(half):
            return slice(half * BANK, (half + 1) * BANK)

        turned_ps, g0_ps, self_ps = work_ps[:], side_acc, lead_acc[:, 1]

        early_tiles = [g_all[:, 1, (CHUNKS - PER_TILE * (v + 1)) * R:(CHUNKS - PER_TILE * v) * R].rearrange(
            "p (s r) -> p s r", r=R) for v in range(TILES)]

        def slab_of(blk, u):
            tile = early_tiles[u // PER_TILE] if blk.chunk == EARLY else a_ring[:, u // PER_TILE]
            return tile[:, u % PER_TILE]

        def x1_place(c):
            i = chunks[c][1]
            return g_all[:, 0, chunk_cols(i + 2)] if i < FETCHED else x_buf[:, i % 2]

        def last_block(c):
            return SLABS * (starts[c + 1] - starts[c] - 1)

        def chunk_cols(i):
            return slice(i * R, (i + 1) * R)

        def side_chunks(c):
            return sum(1 for _, _, runs in chunks[:c] if has_side(runs))

        def splits_g(c):
            return c <= 2 * CHUNKS

        def run_chunk(eng, c, one_block):
            sweep, _, runs = chunks[c]
            n, extras = starts[c], extras_before[c]
            extra_rows = None
            for count, blocks in runs:
                t = 0
                while t < count and (n - starts[c] < straight_blocks(c) or count - t == 1
                                     or blocks[0][-1] == SIDE_ONLY):
                    for rows, d_rows, j, dj, kind in blocks:
                        rows += d_rows * t
                        one_block(Block(c, rows, j + dj * t, n, kind, g_count(sweep, j, kind) + abs(dj) * t,
                                        extras, extra_rows, (n - starts[c]) * SLABS))
                        n, extras = n + 1, extras + (kind == EXTRA)
                        extra_rows = rows if kind == EXTRA else None
                    t += 1
                if t == count:
                    continue
                per_turn = sum(blk[-1] == EXTRA for blk in blocks)
                with eng.Fori(0, count - t) as k:
                    for q, (rows, d_rows, j0, dj, kind) in enumerate(blocks):
                        if d_rows:
                            rows = k + (rows + t)
                        j = j0 if dj == 0 else k + (j0 + t) if dj > 0 else k * -1 + (j0 - t)
                        needed = g_count(sweep, j0, kind)
                        one_block(Block(c, rows, j, k * len(blocks) + (n + q), kind,
                                        k + (needed + t) if dj else needed,
                                        k + extras if per_turn else extras, extra_rows, None))
                        extras += kind == EXTRA
                        extra_rows = rows if kind == EXTRA else None
                n += (count - t) * len(blocks)
                extras += (count - t - 1) * per_turn

        @block.sync
        def _(sp):
            def load_block(blk):
                if blk.chunk == EARLY:
                    return
                for v in range(TILES):
                    if blk.chunk > 0 or blk.slab > 0:
                        last = 2 if blk.chunk == EARLY + 1 else 1
                        sp.wait_ge(rest_ready, blk.n * SLABS + (PER_TILE * (v + 1) - SLABS * last))
                    sp.dma_start(a_ring[:, v], adj_t[bass.ds(blk.rows * TILES_OF_ROWS + blk.j * TILES + v, 1)].rearrange(
                        "o p s r -> p (o s) r")).then_inc(tile_loaded[v], 16)

            for i in range(3):
                sp.dma_start(x_norm[:, chunk_cols(i)], x_rows[i]).then_inc(rows_loaded[i], 16)
            sp.dma_start(w0_sb[:], w0_t.rearrange("(s p) f -> p s f", p=P)).then_inc(consts_loaded, 16)
            sp.dma_start(w1_sb[:], w1).then_inc(consts_loaded, 16)
            sp.dma_start(w2_sb[:], w2).then_inc(consts_loaded, 16)
            for q, b in enumerate((b0, b1, b2)):
                sp.dma_start(biases[:, q:q + 1], b).then_inc(consts_loaded, 16)
            sp.dma_start(base[:, chunk_cols(0)], x_t[0]).then_inc(x_t_loaded[0], 16)
            for c in range(len(chunks)):
                run_chunk(sp, c, load_block)

        @block.gpsimd
        def _(pool):
            def add_x1(c):
                pool.wait_ge(h_ready, c - CHUNKS + 1)
                if chunks[c][1] < FETCHED:
                    pool.wait_ge(x1_back[chunks[c][1]], 16)
                nc.gpsimd.tensor_tensor(h_bufs[c % 2][:], h_bufs[c % 2][:], x1_place(c), ALU.add
                                        ).then_inc(out_ready, 1)

            nc.gpsimd.memset(identity[:], 0.0).then_inc(diagonals, 1)
            nc.gpsimd.memset(centring[:], -1.0 / F).then_inc(diagonals, 1)
            pool.wait_ge(diagonals, 2)
            for square, on_diagonal in ((identity, 1.0), (centring, 1.0 - 1.0 / F)):
                nc.gpsimd.affine_select(out=square[:], in_=square[:], compare_op=ALU.not_equal, fill=on_diagonal,
                                        base=0, pattern=[[-1, P]], channel_multiplier=1)
            nc.gpsimd.memset(mean_col[:], 1.0 / F)
            nc.gpsimd.memset(eps_col[:], EPS)
            nc.gpsimd.memset(zeros[:], 0.0).then_inc(consts_set, 1)
            for i in range(1, CHUNKS):
                if i >= 3:
                    pool.wait_ge(g_saved, i - 2)
                    pool.dma_start(x_norm[:, chunk_cols(i)], x_rows[i]).then_inc(rows_loaded[i], 16)
                pool.dma_start(base[:, chunk_cols(i)], x_t[i]).then_inc(x_t_loaded[i], 16)
            for i in range(CHUNKS):
                pool.wait_ge(sum_ready, i + 1)
                pool.dma_start(x1_dram[i], x_buf[:, i % 2]).then_inc(x1_stored[i % 2], 16)
            for p in range(2):
                pool.wait_ge(x1_stored[p], 16 * (CHUNKS // 2))
            for j in reversed(range(1, CHUNKS)):
                pool.wait_ge(slab_used, SLABS * (freed[j] + 1))
                if j >= 2:
                    pool.dma_start(g_all[:, 0, chunk_cols(j)], x1_dram[j - 2]).then_inc(x1_back[j - 2], 16)
                if j == 1 or j % PER_TILE == 0:
                    v = (CHUNKS - 1 - j) // PER_TILE
                    pool.dma_start(early_tiles[v], adj_t[chunks[EARLY][1] * TILES_OF_ROWS + v]
                                   ).then_inc(early_loaded[v], 16)
            for c in range(2 * CHUNKS, len(chunks)):
                if c < len(chunks) - 1:
                    add_x1(c)
                    pool.wait_ge(out_ready, c - 2 * CHUNKS + 1)
                else:
                    pool.wait_ge(last_out_ready, 1)
                pool.dma_start(out_t[chunks[c][1]], h_bufs[c % 2][:]).then_inc(out_stored[c % 2], 16)
            for p in range(2):
                pool.wait_ge(out_stored[p], 16 * (CHUNKS // 2))

        @block.scalar
        def _(act):
            def deviation(k, variances):
                nc.scalar.activation(dev[:, k % 2], variances, ACT.Sqrt, bias=eps_col[:, 0:1]).then_inc(dev_ready, 1)

            def row_deviation(i):
                act.wait_ge(var_ready, i + 1)
                deviation(i, mean_var[:, i % 2, :, 1])

            def norm_rows(i, slabs):
                act.wait_ge(shift_ready, i + 1)
                for s in slabs:
                    rows = x_norm[:, i * R + s * F:i * R + (s + 1) * F]
                    a = nc.scalar.activation(rows, rows, ACT.Relu, bias=shift[:, s:s + 1], scale=inv[:, s:s + 1])
                if s == SLABS - 1:
                    a.then_inc(rows_normed, 1)

            def save_h0(i):
                act.wait_ge(turned, i + 1)
                if i >= 2:
                    act.wait_ge(self_product, i - 1)
                nc.scalar.activation(h_bufs[i % 2][:], turned_ps, ACT.Copy).then_inc(h0_ready, 1)

            def save_g0(i):
                act.wait_ge(g_product, i + 1)
                nc.scalar.activation(g_all[:, 0, chunk_cols(i)], g0_ps[:], ACT.Copy).then_inc(g_saved, 1)

            def relu_and_squares(c):
                act.wait_ge(centred, c + 1)
                nc.scalar.activation(h_buf[:], work_ps[:], ACT.Relu)
                nc.scalar.activation(squares[:], work_ps[:], ACT.Square).then_inc(squares_ready, 1)

            def x1_deviation(c):
                act.wait_ge(x1_var_ready, c + 1)
                deviation(CHUNKS + c, work_ps[:, 0:SLABS])

            def split_block(blk):
                a, b = places(blk, chunks[blk.chunk][0])
                for u in range(SLABS):
                    if u % PER_TILE == 0:
                        if blk.chunk == EARLY:
                            act.wait_ge(early_loaded[u // PER_TILE], 16)
                        else:
                            act.wait_ge(tile_loaded[u // PER_TILE], blk.n * 16 + (16 if blk.chunk < EARLY else 0))
                    if blk.chunk > 0 or blk.slab > 0 or u >= DEPTH:
                        act.wait_ge(slab_used, blk.n * SLABS + (u + 1 - DEPTH))
                    nc.scalar.activation(a_high[:, u % DEPTH], slab_of(blk, u), ACT.Copy).then_inc(high_ready, 1)
                    if u % HALF == 0 and splits_g(blk.chunk):
                        if u == 0:
                            act.wait_ge(g_saved, blk.g_needed)
                        nc.scalar.activation(
                            g_high[:, a:b, u:u + HALF].rearrange("p g s f -> p g (s f)"),
                            g_all[:, a:b, bass.ds(blk.j * R + u * F, HALF * F)], ACT.Copy
                        ).then_inc(g_high_ready, 1)
                    if blk.slab is not None:
                        steps_after(blk.chunk, blk.slab + u)

            def save_side(c):
                sweep, i, runs = chunks[c]
                if has_side(runs):
                    act.wait_ge(slab_used, SLABS * (starts[c + 1] - ends_with_extra(c)))
                    if sweep == 1:
                        act.wait_ge(sum_ready, c + 1)
                    nc.scalar.activation(part[:, chunk_cols(i)], side_acc[:], ACT.Copy).then_inc(side_saved, 1)

            def relu(c):
                act.wait_ge(sum_ready, c + 1)
                h = h_bufs[c % 2] if c >= 2 * CHUNKS else h_buf
                if c >= 2 * CHUNKS + 2:
                    act.wait_ge(out_stored[c % 2], 16 * (c // 2 - CHUNKS))
                q = chunks[c][0]
                nc.scalar.activation(h[:], total[:], ACT.Relu, bias=biases[:, q:q + 1]).then_inc(h_ready, 1)

            def steps_after(c, slab):
                if c == 0:
                    b, u = slab // SLABS, slab % SLABS
                    if u == 1 and b + 2 < CHUNKS:
                        norm_rows(b + 2, range(HALF))
                    if u == 2 and b + 2 < CHUNKS:
                        norm_rows(b + 2, range(HALF, SLABS))
                    if u == 3 and b + 1 < CHUNKS:
                        save_g0(b + 1)
                    if u == 6 and b + 2 < CHUNKS:
                        save_h0(b + 2)
                    if u == 7 and b + 3 < CHUNKS:
                        row_deviation(b + 3)
                elif c < CHUNKS:
                    if slab == 5:
                        save_side(c - 1)
                    if slab == 7:
                        relu_and_squares(c - 1)
                    if slab == 12:
                        x1_deviation(c - 1)
                    if c == CHUNKS - 1 and slab == late_slab + 7:
                        relu_and_squares(c)
                    if c == CHUNKS - 1 and slab == late_slab + 12:
                        x1_deviation(c)
                elif c == CHUNKS:
                    if slab == 5:
                        save_side(c - 1)
                else:
                    if slab == (8 if ends_with_extra(c - 1) else 4 if c <= 2 * CHUNKS else 6):
                        relu(c - 1)
                    if slab == 5 and not ends_with_extra(c - 1):
                        save_side(c - 1)
                    if ends_with_extra(c) and slab == last_block(c) + 5:
                        save_side(c)

            act.wait_ge(consts_set, 1)
            nc.scalar.activation(table_ready[:], eps_col[:], ACT.Sqrt)
            row_deviation(0)
            norm_rows(0, range(SLABS))
            row_deviation(1)
            save_h0(0)
            norm_rows(1, range(SLABS))
            row_deviation(2)
            save_g0(0)
            save_h0(1)
            for c in range(len(chunks)):
                if c == 1:
                    act.wait_ge(consts_loaded, 16 * 6)
                run_chunk(act, c, split_block)
            relu(len(chunks) - 1)

        @block.vector
        def _(dve):
            def row_stats(i):
                dve.wait_ge(rows_loaded[i], 16)
                if i:
                    dve.wait_ge(var_ready, i)
                for s in range(SLABS):
                    bn = nc.vector.bn_stats(stats[:, s], x_norm[:, i * R + s * F:i * R + (s + 1) * F])
                bn.then_inc(stats_ready, 1)
                dve.wait_ge(stats_ready, i + 1)
                if i >= 2:
                    dve.wait_ge(dev_ready, i - 1)
                for s in range(SLABS):
                    bn = nc.vector.bn_aggr(mean_var[:, i % 2, s], stats[:, s])
                bn.then_inc(var_ready, 1)

            def invert(k):
                dve.wait_ge(dev_ready, k + 1)
                nc.vector.reciprocal(inv[:], dev[:, k % 2]).then_inc(inv_ready, 1)
                dve.wait_ge(inv_ready, k + 1)

            def row_shift(i):
                if i:
                    dve.wait_ge(rows_normed, i)
                invert(i)
                nc.vector.scalar_tensor_tensor(out=shift[:], in0=mean_var[:, i % 2, :, 0], scalar=-1.0, in1=inv[:],
                                               op0=ALU.mult, op1=ALU.mult).then_inc(shift_ready, 1)

            def add_base(i):
                dve.wait_ge(x_t_loaded[i], 16)
                dve.wait_ge(self_product, i + 1)
                nc.vector.scalar_tensor_tensor(out=base[:, chunk_cols(i)], in0=self_ps,
                                               scalar=biases[:, 0:1], in1=base[:, chunk_cols(i)],
                                               op0=ALU.add, op1=ALU.add).then_inc(base_saved, 1)

            def save_g1(c):
                invert(CHUNKS + c)
                dve.wait_ge(g_product, CHUNKS + c + 1)
                nc.vector.tensor_tensor(
                    g_all[:, 1, chunk_cols(c)].rearrange("p (s f) -> p s f", f=F),
                    work_ps[:].rearrange("p (s f) -> p s f", f=F),
                    inv[:].unsqueeze(2).to_broadcast([P, SLABS, F]), ALU.mult).then_inc(g_saved, 1)

            def save_g2(c):
                dve.wait_ge(g_product, CHUNKS + c + 1)
                nc.vector.tensor_copy(g_all[:, 0, chunk_cols(chunks[c][1])], work_ps[:]).then_inc(g_saved, 1)

            def split_block(blk):
                a, b = places(blk, chunks[blk.chunk][0])
                for u in range(SLABS):
                    dve.wait_ge(high_ready, blk.n * SLABS + (u + 1))
                    rest = nc.vector.tensor_tensor(a_rest[:, u % DEPTH], slab_of(blk, u),
                                                   a_high[:, u % DEPTH].bitcast(F32), ALU.subtract)
                    if u % HALF == 0 and splits_g(blk.chunk):
                        dve.wait_ge(g_high_ready, blk.n * 2 + (u // HALF + 1))
                        rest = nc.vector.tensor_tensor(
                            g_rest[:, a:b, u:u + HALF].rearrange("p g s f -> p g (s f)"),
                            g_all[:, a:b, bass.ds(blk.j * R + u * F, HALF * F)],
                            g_high[:, a:b, u:u + HALF].rearrange("p g s f -> p g (s f)").bitcast(F32),
                            ALU.subtract)
                    rest.then_inc(rest_ready, 1)
                    if blk.slab is not None:
                        steps_after(blk.chunk, blk.slab + u)
                    if u == 3 and blk.extra_rows is not None:
                        save_extra(blk.extra_rows, blk.chunk, blk.n, blk.extras)

            def finish_sum(c):
                sweep, i, _ = chunks[c]
                dve.wait_ge(slab_used, SLABS * lead_ends[c])
                acc = lead_acc[:, c % 2]
                if sweep == 0:
                    dve.wait_ge(base_saved, CHUNKS)
                    if i >= 2:
                        dve.wait_ge(x1_stored[i % 2], 16 * (i // 2))
                    nc.vector.tensor_tensor(x_buf[:, i % 2], acc, base[:, chunk_cols(i)], ALU.add
                                            ).then_inc(sum_ready, 1)
                elif sweep == 1 and i == 0:
                    nc.vector.tensor_copy(total[:], acc).then_inc(sum_ready, 1)
                else:
                    dve.wait_ge(side_saved, side_chunks(CHUNKS) if sweep == 1 else side_chunks(2 * CHUNKS))
                    if sweep == 2:
                        dve.wait_ge(extra_saved, extras_before[-1])
                    nc.vector.tensor_tensor(total[:], acc, part[:, chunk_cols(i)], ALU.add).then_inc(sum_ready, 1)

            def save_extra(rows, c, n, number):
                dve.wait_ge(slab_used, n * SLABS)
                where = part[:, bass.ds(rows * R, R)]
                if c == CHUNKS + 1:
                    nc.vector.tensor_copy(where, work_ps[:]).then_inc(extra_saved, 1)
                else:
                    dve.wait_ge(side_saved, side_chunks(c))
                    dve.wait_ge(extra_saved, number + -1)
                    nc.vector.tensor_tensor(where, work_ps[:], where, ALU.add).then_inc(extra_saved, 1)

            def last_result():
                c = len(chunks) - 1
                dve.wait_ge(h_ready, c - CHUNKS + 1)
                dve.wait_ge(x1_back[chunks[c][1]], 16)
                nc.vector.tensor_tensor(h_bufs[c % 2][:], h_bufs[c % 2][:], x1_place(c), ALU.add
                                        ).then_inc(last_out_ready, 1)

            def steps_after(c, slab):
                if c == 0:
                    b, u = slab // SLABS, slab % SLABS
                    if u == 3 and b + 3 < CHUNKS:
                        row_stats(b + 3)
                    if u == 5 and b + 1 < CHUNKS:
                        add_base(b + 1)
                    if u == 7 and b + 3 < CHUNKS:
                        row_shift(b + 3)
                elif c != CHUNKS:
                    if slab == 3 and not ends_with_extra(c - 1):
                        finish_sum(c - 1)
                    if slab == 15 and c < CHUNKS:
                        save_g1(c - 1)
                    if c == CHUNKS - 1 and slab == late_slab + 3:
                        finish_sum(c)
                    if c == CHUNKS - 1 and slab == late_slab + 15:
                        save_g1(c)
                    if ends_with_extra(c) and slab == last_block(c) + 3:
                        finish_sum(c)
                    if CHUNKS < c <= 2 * CHUNKS:
                        if slab == 8 and ends_with_extra(c - 1):
                            save_extra(CHUNKS - 1, c - 1, starts[c], extras_before[c])
                        if slab == (12 if ends_with_extra(c - 1) else 7):
                            save_g2(c - 1)

            for i in range(3):
                row_stats(i)
                row_shift(i)
            dve.wait_ge(consts_loaded, 16 * 6)
            add_base(0)
            for c in range(len(chunks)):
                run_chunk(dve, c, split_block)
            finish_sum(len(chunks) - 1)
            last_result()

        @block.tensor
        def _(pe):
            def turn(i):
                pe.wait_ge(rows_normed, i + 1)
                if i:
                    pe.wait_ge(h0_ready, i)
                for s in range(SLABS):
                    mm = nc.tensor.transpose(turned_ps[:, s * P:(s + 1) * P],
                                             x_norm[:, i * R + s * F:i * R + (s + 1) * F], identity[:])
                mm.then_inc(turned, 1)

            def g0(i):
                pe.wait_ge(h0_ready, i + 1)
                if i:
                    pe.wait_ge(g_saved, i)
                make_g(g0_ps, h_bufs[i % 2], w0_sb[:, 1])

            def self_term(i):
                if i:
                    pe.wait_ge(base_saved, i)
                for half in range(HALVES):
                    mm = nc.tensor.matmul(self_ps[:, cols(half)], w0_sb[:, 0], h_bufs[i % 2][:, cols(half)],
                                          start=True, stop=True)
                mm.then_inc(self_product, 1)

            def centre(c):
                pe.wait_ge(sum_ready, c + 1)
                pe.wait_ge(g_saved, CHUNKS + c)
                for half in range(HALVES):
                    mm = nc.tensor.matmul(work_ps[:, cols(half)], centring[:], x_buf[:, c % 2, cols(half)],
                                          start=True, stop=True)
                mm.then_inc(centred, 1)

            def x1_variance(c):
                pe.wait_ge(squares_ready, c + 1)
                for s in range(SLABS):
                    mm = nc.tensor.matmul(work_ps[:, s:s + 1], squares[:, s * P:(s + 1) * P], mean_col[:],
                                          start=True, stop=True)
                mm.then_inc(x1_var_ready, 1)

            def make_g(out, h, weights):
                for s in range(SLABS):
                    mm = nc.tensor.matmul(out[:, s * F:(s + 1) * F], h[:, s * P:(s + 1) * P], weights,
                                          start=True, stop=True)
                mm.then_inc(g_product, 1)

            def open_acc(acc):
                for half in range(HALVES):
                    nc.tensor.matmul(acc[:, half * BANK:half * BANK + 2], zeros[:], zeros[:, 0:2],
                                     start=True, stop=False, skip_group_check=True)

            def product_block(blk):
                c = blk.chunk
                sweep = chunks[c][0]
                if blk.kind == LEAD_ONLY:
                    accs = [(LEAD[sweep], lead_acc[:, c % 2])]
                elif blk.kind == SHARED:
                    accs = [(LEAD[sweep], lead_acc[:, c % 2]), (SIDE[sweep], side_acc[:])]
                else:
                    accs = [(SIDE[sweep], side_acc[:] if blk.kind == SIDE_ONLY else work_ps[:])]
                if blk.slab == 0:
                    if c >= 2:
                        pe.wait_ge(sum_ready, c - 1)
                    open_acc(lead_acc[:, c % 2])
                if blk.kind == SHARED and blk.slab == first_shared[c]:
                    if side_chunks(c):
                        pe.wait_ge(side_saved, side_chunks(c))
                    open_acc(side_acc[:])
                if blk.kind == EXTRA:
                    pe.wait_ge(g_saved, blk.g_needed)
                    if c > CHUNKS + 1:
                        pe.wait_ge(extra_saved, blk.extras)
                for u in range(SLABS):
                    pe.wait_ge(rest_ready, blk.n * SLABS + (u + 1))
                    for g, acc in accs:
                        for w, a in ((g_high, a_high), (g_high, a_rest), (g_rest, a_high)):
                            for half in range(HALVES):
                                mm = nc.tensor.matmul(
                                    acc[:, cols(half)], w[:, g, u], a[:, u % DEPTH, cols(half)],
                                    start=blk.kind == EXTRA and u == 0 and (w, a) == (g_high, a_high),
                                    stop=False, skip_group_check=True)
                    mm.then_inc(slab_used, 1)
                    if blk.slab is not None:
                        steps_after(c, blk.slab + u)

            def g1(c):
                pe.wait_ge(dev_ready, CHUNKS + c + 1)
                make_g(work_ps, h_buf, w1_sb[:])

            def g2(c):
                pe.wait_ge(h_ready, c - CHUNKS + 1)
                pe.wait_ge(g_saved, CHUNKS + c)
                if extras_before[c + 1]:
                    pe.wait_ge(extra_saved, extras_before[c + 1])
                make_g(work_ps, h_buf, w2_sb[:])

            def steps_after(c, slab):
                if c == 0:
                    b, u = slab // SLABS, slab % SLABS
                    if u == 1 and b + 1 < CHUNKS:
                        self_term(b + 1)
                    if u == 3 and b + 2 < CHUNKS:
                        turn(b + 2)
                    if u == 7 and b + 2 < CHUNKS:
                        g0(b + 2)
                elif c < CHUNKS:
                    if slab == 2:
                        centre(c - 1)
                    if slab == 7:
                        x1_variance(c - 1)
                    if slab == 11:
                        g1(c - 1)
                    if c == CHUNKS - 1 and slab == late_slab + 2:
                        centre(c)
                    if c == CHUNKS - 1 and slab == late_slab + 7:
                        x1_variance(c)
                    if c == CHUNKS - 1 and slab == late_slab + 11:
                        g1(c)
                elif CHUNKS < c <= 2 * CHUNKS:
                    if slab == (10 if ends_with_extra(c - 1) else 4):
                        g2(c - 1)

            pe.wait_ge(consts_set, 1)
            turn(0)
            pe.wait_ge(consts_loaded, 16 * 6)
            g0(0)
            self_term(0)
            turn(1)
            g0(1)

            for c in range(len(chunks)):
                if c == 1:
                    pe.wait_ge(h0_ready, CHUNKS)
                    pe.wait_ge(g_saved, CHUNKS)
                    pe.wait_ge(base_saved, CHUNKS)
                run_chunk(pe, c, product_block)


def kernel(x, adj, L0_gnn_W, L0_gnn_b, L1_gnn_W1, L1_gnn_b1, L1_gnn_W2, L1_gnn_b2):
    import numpy as np
    import concourse.bacc as bacc
    from concourse.bass_utils import run_bass_kernel_spmd

    adj_t = np.asarray(adj).reshape(CHUNKS, R, TILES_OF_ROWS, PER_TILE, P).transpose(0, 2, 4, 3, 1)
    adj_t = adj_t.reshape(CHUNKS * TILES_OF_ROWS, P, PER_TILE, R)
    arrays = {
        "adj_t": adj_t,
        "x_rows": np.asarray(x).reshape(CHUNKS, SLABS, P, F).transpose(0, 2, 1, 3).reshape(CHUNKS, P, R),
        "x_t": np.asarray(x).reshape(CHUNKS, R, F).transpose(0, 2, 1),
        "w0_t": np.asarray(L0_gnn_W).T,
        "b0": np.asarray(L0_gnn_b).reshape(F, 1),
        "w1": np.asarray(L1_gnn_W1),
        "b1": np.asarray(L1_gnn_b1).reshape(F, 1),
        "w2": np.asarray(L1_gnn_W2),
        "b2": np.asarray(L1_gnn_b2).reshape(F, 1),
    }
    arrays = {k: np.ascontiguousarray(v) for k, v in arrays.items()}

    nc = bacc.Bacc("TRN2", target_bir_lowering=False, num_devices=1)
    ins = [nc.dram_tensor(f"in_{k}", v.shape, mybir.dt.from_np(v.dtype), kind="ExternalInput").ap()
           for k, v in arrays.items()]
    out_t = nc.dram_tensor("out_t", [CHUNKS, F, R], F32, kind="ExternalOutput").ap()
    build(nc, *ins, out_t)
    r = run_bass_kernel_spmd(nc, [{f"in_{k}": v for k, v in arrays.items()}], core_ids=[0])
    return np.ascontiguousarray(r.results[0]["out_t"].transpose(0, 2, 1)).reshape(N, F)
```
